# Optimizing a Trainium2 kernel written in Bass

```python
import numpy as np
import jax
import jax.numpy as jnp

def _softmax(x, axis=-1):
    return jax.nn.softmax(x, axis=axis)

def _gelu(x):
    return jax.nn.gelu(x, approximate=True)

def _silu(x):
    return jax.nn.silu(x)

def _sigmoid(x):
    return jax.nn.sigmoid(x)

def _layernorm(x, axis=-1, eps=1e-05):
    m = jnp.mean(x, axis=axis, keepdims=True)
    v = jnp.var(x, axis=axis, keepdims=True)
    return (x - m) / jnp.sqrt(v + eps)

def _scatter_add(tgt, idx, src, axis=0):
    return tgt.at[idx].add(src)

def _segment_sum(src, seg, n):
    return jax.ops.segment_sum(src, seg, n)
kernel_name = 'mk_adj_resnorm_d1_adj_r2_999eee'

def setup_inputs(seed: int=0):
    np.random.seed(seed)
    _w = jnp.asarray

    def _rec_inputs():
        import jax
        import jax.numpy as jnp
        _gk = jax.random.key(seed)
        x = -0.001003 + 1 * jax.random.normal(jax.random.fold_in(_gk, 1), (6144, 128), jnp.float32)
        _w = (1.0 + jnp.arange(6144, dtype=jnp.float32)) ** (-0.5)
        _w = _w / _w.mean()
        _pij = jnp.clip(0.000651042 * _w[:, None] * _w[None, :], 0.0, 1.0)
        _a = jax.random.uniform(jax.random.fold_in(_gk, 2), (6144, 6144)) < _pij
        adj = _a.astype(jnp.int32)
        return (x, adj)
    x, adj = _rec_inputs()

    def _L0_gnn_setup():
        import jax, jax.numpy as jnp
        import numpy as np
        M = 6144
        N = 6144
        D = 128
        TEMPERATURE = 0.07
        NEG_PAD = jnp.float32(-2 ** 32 + 1)
        key = jax.random.key(seed)
        k1, k2, k3, k4 = jax.random.split(key, 4)
        xx_anchor = jax.random.normal(k1, (M, D), dtype=jnp.float32)
        inp = jax.random.normal(k2, (N, D), dtype=jnp.float32)
        adj = (jax.random.uniform(k3, (M, N)) < 0.002).astype(jnp.int32)
        limit = jnp.sqrt(6.0 / (D + D)).astype(jnp.float32)
        weight = jax.random.uniform(k4, (D, D), minval=-limit, maxval=limit, dtype=jnp.float32)
        return {'xx_anchor': xx_anchor, 'input': inp, 'adj': adj, 'weight': weight}
    _L0_gnn_all = _L0_gnn_setup()
    _L0_gnn_in = {k: v for k, v in _L0_gnn_all.items() if k in ('input', 'weight')}
    del _L0_gnn_all
    return {'x': x, 'adj': adj, 'L0_gnn_input': _L0_gnn_in['input'], 'L0_gnn_weight': _L0_gnn_in['weight']}

def reference(x, adj, L0_gnn_input, L0_gnn_weight):
    import jax
    import jax.numpy as jnp

    def _L0_gnn_ref(xx_anchor, input, adj, weight):
        import jax, jax.numpy as jnp
        import numpy as np
        M = 6144
        N = 6144
        D = 128
        TEMPERATURE = 0.07
        NEG_PAD = jnp.float32(-2 ** 32 + 1)
        anchor_adj = jnp.einsum('md,de,ne->mn', xx_anchor, weight, input)
        scores = jnp.where(adj > 0, anchor_adj, NEG_PAD)
        atten = jax.nn.softmax(scores / TEMPERATURE, axis=1)
        return atten @ input
    x = _layernorm(x + _L0_gnn_ref(x, L0_gnn_input, adj, L0_gnn_weight), axis=-1)
    return x

_drawn_inputs = setup_inputs


def setup_inputs(seed=0):
    import zlib

    import numpy as np

    out = dict(_drawn_inputs(seed))
    spreads = {}
    factors = {}
    for name, (base, spread) in spreads.items():
        noise = np.random.default_rng([zlib.crc32(name.encode()), seed]).standard_normal(out[name].shape)
        drawn = base * np.exp(spread * noise) if base else spread * noise
        out[name] = jnp.asarray(drawn.astype(out[name].dtype))
    for name, factor in factors.items():
        out[name] = (out[name] * factor).astype(out[name].dtype)
    return out
```

```python
from contextlib import ExitStack

import concourse.bass as bass
from concourse import mybir

F32 = mybir.dt.float32
F32R = mybir.dt.float32r
I32 = mybir.dt.int32
ALU = mybir.AluOpType
ACT = mybir.ActivationFunctionType
AX_X = mybir.AxisListType.X

TEMPERATURE = 0.07
EPS = 1e-5
BIG = 2.0**100
P = 128


def gnn_attention_norm(nc, x, x_t, adj, values, keys_t, weight, out):
    rows, d = x.shape
    cols = values.shape[0]
    assert d == P and rows % (2 * P) == 0

    CHUNK = 1024
    HALF = 512
    CHUNKS = cols // CHUNK
    PAIRS = rows // (2 * P)
    UNITS = 2 * CHUNKS
    ALL_UNITS = UNITS * PAIRS
    STEPS = cols // 256
    CHUNK_STEPS = CHUNK // 256
    VALUES = CHUNK // P
    ALL_STEPS = STEPS * PAIRS
    SLOTS = 9
    AHEAD = 2
    LEAD = UNITS + AHEAD
    LAG = 2
    TURNED = 4
    BANKS = 3
    ROUND = 3
    ROUND_STEPS = ROUND * STEPS
    ROUNDS = PAIRS // ROUND
    EXTRA = 6
    START = 20
    BANK_USES = STEPS + 1
    SCALE = 1.0 / TEMPERATURE
    assert (ROUND * BANK_USES) % BANKS == 0 and (ROUND * CHUNKS) % SLOTS == 0
    assert ROUND_STEPS % TURNED == 0 and PAIRS % ROUND == 0

    def use(r):
        return r + (r + STEPS - EXTRA) // STEPS

    def extra_use(p):
        return use(STEPS * p + EXTRA) - 1

    values_v = values.rearrange("(b p) n -> p b n", p=P)

    def rows_of(dram, p):
        return dram[bass.ds(p * 2 * P, 2 * P), :]

    with ExitStack() as ctx:

        def sb(name, shape, dt):
            return ctx.enter_context(nc.sbuf_tensor(name, shape, dt))

        def psum(name, shape):
            return ctx.enter_context(nc.psum_tensor(name, shape, F32))

        def sem(name):
            return ctx.enter_context(nc.semaphore(name))

        keys_hi = sb("keys_hi", [P, cols], F32R)
        keys_lo = sb("keys_lo", [P, cols], F32R)
        values_hi = sb("values_hi", [P, cols // P, P], F32R)
        values_lo = sb("values_lo", [P, cols // P, P], F32R)
        ring = sb("ring", [P, SLOTS, 2, CHUNK], I32)
        turned = sb("turned", [P, TURNED, 2, 2, 2 * P], F32R)
        query_hi = sb("query_hi", [P, ROUND, 2 * P], F32R)
        query_lo = sb("query_lo", [P, ROUND, 2 * P], F32R)
        raw_values = sb("raw_values", [P, VALUES, P], F32)
        weight_sb = sb("weight_sb", [P, P], F32)
        identity = sb("identity", [P, P], F32)
        xt_sb = sb("xt_sb", [P, ROUND, 2 * P], F32)
        x_sb = sb("x_sb", [P, ROUND, 2, P], F32)
        out_sb = sb("out_sb", [P, ROUND, 2, P], F32)
        sum_low = sb("sum_low", [P, 2 * P], F32)
        summed_t = sb("summed_t", [P, 2 * P], F32)
        unit_max = sb("unit_max", [P, ROUND, 2, CHUNKS], F32)
        unit_sum = sb("unit_sum", [P, ROUND, 2, CHUNKS], F32)
        row_max = sb("row_max", [P, ROUND, 2], F32)
        exp_bias = sb("exp_bias", [P, ROUND, 2], F32)
        denom = sb("denom", [P, ROUND, 2], F32)
        inv_denom = sb("inv_denom", [P, ROUND, 2], F32)
        stats = sb("stats", [P, ROUND, 2, 6], F32)
        mean_var = sb("mean_var", [P, ROUND, 2, 2], F32)
        var_eps = sb("var_eps", [P, ROUND, 2], F32)
        inv_std = sb("inv_std", [P, ROUND, 2], F32)
        minus_half = sb("minus_half", [P, 2], F32)
        eps = sb("eps", [P, 2], F32)

        score_ps = [psum(f"score_ps{i}", [P, CHUNK]) for i in range(2)]
        turn_ps = [psum(f"turn_ps{i}", [P, HALF]) for i in range(BANKS)]
        sum_ps = psum("sum_ps", [P, 2, 2 * P])

        raw = ring[:, CHUNKS:SLOTS, :, :].bitcast(F32).rearrange("p s a n -> p (s a n)")

        weight_landed = sem("weight_landed")
        raw_keys_landed = [sem(f"raw_keys_landed{c}") for c in range(CHUNKS)]
        raw_values_landed = sem("raw_values_landed")
        adj_landed = [sem(f"adj_landed{s}") for s in range(SLOTS)]
        xt_landed = [sem(f"xt_landed{i}") for i in range(ROUND)]
        x_landed = [sem(f"x_landed{i}") for i in range(ROUND)]
        out_free = [sem(f"out_free{i}") for i in range(ROUND)]
        consts_ready = sem("consts_ready")
        keys_hi_ready = sem("keys_hi_ready")
        keys_ready = sem("keys_ready")
        values_hi_ready = sem("values_hi_ready")
        values_ready = sem("values_ready")
        queries_made = sem("queries_made")
        query_hi_ready = sem("query_hi_ready")
        query_ready = sem("query_ready")
        scores_made = sem("scores_made")
        mask_ready = sem("mask_ready")
        masked = sem("masked")
        row_max_ready = sem("row_max_ready")
        exp_bias_ready = sem("exp_bias_ready")
        exp_done = sem("exp_done")
        turns_made = sem("turns_made")
        turned_hi = sem("turned_hi")
        turned_both = sem("turned_both")
        steps_summed = sem("steps_summed")
        sum_low_copied = sem("sum_low_copied")
        sum_copied = sem("sum_copied")
        denom_ready = sem("denom_ready")
        inv_denom_ready = sem("inv_denom_ready")
        y_ready = sem("y_ready")
        stats_ready = sem("stats_ready")
        mean_var_ready = sem("mean_var_ready")
        identity_cleared = sem("identity_cleared")
        var_eps_ready = sem("var_eps_ready")
        inv_std_ready = sem("inv_std_ready")
        normed = sem("normed")

        def unit(g):
            return ring[:, g // 2 % SLOTS, g % 2, :].bitcast(F32)

        block = ctx.enter_context(nc.Block())

        @block.sync
        def _(sp):
            sp.dma_start(weight_sb[:, :], weight).then_inc(weight_landed, 16)

            def load_xt(p, i):
                sp.dma_start(xt_sb[:, i, :], x_t[:, bass.ds(p * 2 * P, 2 * P)]).then_inc(xt_landed[i], 16)

            def load_x(p, i):
                src = rows_of(x, p).rearrange("(a p) n -> p a n", p=P)
                sp.dma_start(x_sb[:, i, :, :], src).then_inc(x_landed[i], 16)

            def load_adj(p, k):
                c = k % CHUNKS
                src = rows_of(adj, p)[:, c * CHUNK : (c + 1) * CHUNK].rearrange("(a p) n -> p a n", p=P)
                sp.dma_start(ring[:, k % SLOTS, :, :], src).then_inc(adj_landed[k % SLOTS], 16)

            def store(p, i, count):
                sp.wait_ge(normed, count)
                dst = rows_of(out, p).rearrange("(a p) n -> p a n", p=P)
                sp.dma_start(dst, out_sb[:, i, :, :]).then_inc(out_free[i], 16)

            def load_values(c):
                if c:
                    sp.wait_ge(values_ready, c)
                sp.dma_start(raw_values[:, :, :],
                             values_v[:, c * VALUES : (c + 1) * VALUES, :]).then_inc(raw_values_landed, 16)

            load_xt(0, 0)
            for c in range(CHUNKS):
                sp.dma_start(raw[:, c * CHUNK : (c + 1) * CHUNK],
                             keys_t[:, c * CHUNK : (c + 1) * CHUNK]).then_inc(raw_keys_landed[c], 16)
                load_adj(0, c)
                if c == 0:
                    load_xt(1, 1)
            for i in range(SLOTS - CHUNKS):
                sp.wait_ge(keys_ready, 2 * i + 2)
                load_adj(1, CHUNKS + i)
                if i == 0:
                    load_values(0)
            load_values(1)
            load_xt(2, 2)
            load_x(0, 0)
            load_x(1, 1)

            def chunk(it, i):
                k = SLOTS + i
                p = it * ROUND + k // CHUNKS
                sp.wait_ge(turns_made, it * (ROUND * BANK_USES) + use(CHUNK_STEPS * i + CHUNK_STEPS - 1) + 1)
                load_adj(p, k)

            def pair_io(it, i):
                q, c = divmod(i, CHUNKS)
                p = it * ROUND + q
                static = isinstance(it, int)
                if c == CHUNKS - 2 and not (static and p == 0):
                    store(p - 1, (q - 1) % ROUND, p)
                if c == CHUNKS - 1:
                    if not static or p + 3 < PAIRS:
                        load_xt(p + 3, q % ROUND)
                    if not static or p + 2 < PAIRS:
                        load_x(p + 2, (q + 2) % ROUND)

            body = ROUND * CHUNKS
            first = CHUNKS - 1
            for i in range(first):
                if i + 2 < CHUNKS:
                    load_values(i + 2)
                chunk(0, i)
                pair_io(0, i)
            with sp.Fori(0, ROUNDS - 1) as it:
                for i in range(first, first + body):
                    chunk(it, i)
                    pair_io(it, i)
            for i in range(first, body):
                if (ROUNDS - 1) * body + SLOTS + i < PAIRS * CHUNKS:
                    chunk(ROUNDS - 1, i)
                pair_io(ROUNDS - 1, i)
            store(PAIRS - 1, (PAIRS - 1) % ROUND, PAIRS)
            for i in range(ROUND):
                sp.wait_ge(out_free[i], 16 * (ROUNDS + 1))

        @block.tensor
        def _(pe):
            def scores(it, r, halves=(0, 1)):
                g = LEAD + r // 2
                p, c, t = g // UNITS, g % UNITS // 2, g % 2
                q_hi = query_hi[:, p % ROUND, t * P : (t + 1) * P]
                q_lo = query_lo[:, p % ROUND, t * P : (t + 1) * P]
                for h in halves:
                    if h == 0:
                        if g >= 2:
                            pe.wait_ge(masked, it * ROUND * UNITS + g - 1)
                        if g % UNITS == 0:
                            pe.wait_ge(query_ready, it * ROUND + p + 1)
                    n0 = c * CHUNK + h * HALF
                    k_hi, k_lo = keys_hi[:, n0 : n0 + HALF], keys_lo[:, n0 : n0 + HALF]
                    to = score_ps[g % 2][:, h * HALF : (h + 1) * HALF]
                    pe.matmul(to, q_hi, k_hi, start=True, stop=False)
                    pe.matmul(to, q_hi, k_lo, start=False, stop=False)
                    last = pe.matmul(to, q_lo, k_hi, start=False, stop=True)
                if h == 1:
                    last.then_inc(scores_made, 1)

            def turn(it, r):
                p, q = divmod(r, STEPS)
                c = q // CHUNK_STEPS
                if q % CHUNK_STEPS == 0:
                    pe.wait_ge(exp_done, it * ROUND * UNITS + UNITS * p + 2 * c + 2)
                b = use(r)
                if b - BANKS >= 0:
                    free_bank(it, b - BANKS)
                for i in range(2):
                    n0 = (2 * (q % CHUNK_STEPS) + i) * P
                    for t in range(2):
                        last = pe.transpose(turn_ps[b % BANKS][:, (2 * i + t) * P : (2 * i + t + 1) * P],
                                            unit(UNITS * p + 2 * c + t)[:, n0 : n0 + P], identity[:, :])
                last.then_inc(turns_made, 1)

            def free_bank(it, b):
                p, q = divmod(b, BANK_USES)
                if q == EXTRA:
                    if p == 0:
                        pe.wait_ge(query_ready, 3)
                    else:
                        pe.wait_ge(y_ready, it * ROUND + p)
                else:
                    r = STEPS * p + q - (q > EXTRA)
                    pe.wait_ge(turned_both, it * ROUND_STEPS + r + 1)

            def sum_values(it, r):
                q = r % STEPS
                if q == 0:
                    pe.wait_ge(sum_copied, it * ROUND + r // STEPS)
                pe.wait_ge(turned_both, it * ROUND_STEPS + r + 1)
                if isinstance(it, int) and it == 0 and q % CHUNK_STEPS == 0:
                    pe.wait_ge(values_ready, q // CHUNK_STEPS + 1)
                for i in range(2):
                    probs = turned[:, r % TURNED, i, :, :]
                    n = 2 * q + i
                    first, end = n == 0, n == cols // P - 1
                    pe.matmul(sum_ps[:, :, :], values_hi[:, n, :], probs, start=first, stop=False)
                    last = pe.matmul(sum_ps[:, 0, :], values_lo[:, n, :], probs[:, 0, :], start=False, stop=end)
                last.then_inc(steps_summed, 1)

            def make_query(to, i):
                return pe.matmul(to, weight_sb[:, :], xt_sb[:, i, :], start=True, stop=True)

            def extra(it, p, b, finish, query):
                free_bank(it, b - BANKS)
                to = turn_ps[b % BANKS]
                if query:
                    i = (p + 2) % ROUND
                    pe.wait_ge(xt_landed[i], 16 * (it + (p + 2) // ROUND + 1))
                    last = make_query(to[:, 0 : 2 * P], i)
                if finish:
                    pe.wait_ge(sum_copied, it * ROUND + p)
                    for t in range(2):
                        last = pe.transpose(to[:, (2 + t) * P : (3 + t) * P],
                                            summed_t[:, t * P : (t + 1) * P], identity[:, :])
                last.then_inc(turns_made, 1)

            pe.wait_ge(weight_landed, 16)
            for g in range(LEAD):
                if g in (0, 4):
                    i = g // 4
                    pe.wait_ge(xt_landed[i], 16)
                    make_query(turn_ps[i][:, 0 : 2 * P], i).then_inc(queries_made, 1)
                if g % 2 == 0 and g < UNITS:
                    pe.wait_ge(keys_ready, g // 2 + 1)
                scores(0, 2 * (g - LEAD))
            pe.wait_ge(consts_ready, 2)
            pe.wait_ge(query_ready, 2)

            def step(it, r):
                if not isinstance(it, int) or it * ROUND_STEPS + r < ALL_STEPS:
                    turn(it, r)
                if r % STEPS == LAG + 1:
                    sum_values(it, r - LAG - 1)
                if not isinstance(it, int) or LEAD + (it * ROUND_STEPS + r) // 2 < ALL_UNITS:
                    scores(it, r, (r % 2,))
                if r >= LAG and r % STEPS != LAG:
                    sum_values(it, r - LAG)

            for r in range(START):
                step(0, r)
                if r == EXTRA - 1:
                    extra(0, 0, extra_use(0), False, True)
            pe.wait_ge(values_ready, CHUNKS)
            with pe.Fori(0, ROUNDS - 1) as it:
                for r in range(START, START + ROUND_STEPS):
                    step(it, r)
                    if r % STEPS == EXTRA - 1:
                        extra(it, r // STEPS, extra_use(r // STEPS), True, True)
            for r in range(START, ROUND_STEPS + LAG):
                step(ROUNDS - 1, r)
                if r % STEPS == EXTRA - 1:
                    extra(ROUNDS - 1, r // STEPS, extra_use(r // STEPS), True, False)
            extra(ROUNDS - 1, ROUND, use(ROUND_STEPS), True, False)

        @block.scalar
        def _(act):
            def mask(it, g):
                k = g // 2
                slot = k % SLOTS
                if g % 2 == 0:
                    act.wait_ge(adj_landed[slot], it * 16 * (ROUND * CHUNKS // SLOTS) + 16 * (k // SLOTS + 1))
                nc.scalar.activation(unit(g), ring[:, slot, g % 2, :], ACT.Relu,
                                     bias=BIG, scale=-BIG).then_inc(mask_ready, 1)

            def exp(it, g):
                p, c, t = g // UNITS % ROUND, g % UNITS // 2, g % 2
                if g % UNITS == 0:
                    act.wait_ge(exp_bias_ready, it * ROUND + g // UNITS + 1)
                nc.scalar.activation(unit(g), unit(g), ACT.Exp, bias=exp_bias[:, p, t : t + 1], scale=SCALE,
                                     accum_out=unit_sum[:, p, t, c : c + 1]).then_inc(exp_done, 1)

            def high(it, r):
                b = use(r)
                if r >= TURNED:
                    act.wait_ge(steps_summed, it * ROUND_STEPS + r - TURNED + 1)
                act.wait_ge(turns_made, it * ROUND * BANK_USES + b + 1)
                nc.scalar.activation(turned[:, r % TURNED, :, 0, :],
                                     turn_ps[b % BANKS][:, :].rearrange("p (i n) -> p i n", i=2),
                                     ACT.Copy).then_inc(turned_hi, 1)

            def low_sum(it, p):
                act.wait_ge(steps_summed, it * ROUND_STEPS + STEPS * p)
                nc.scalar.activation(sum_low[:, :], sum_ps[:, 1, :], ACT.Copy).then_inc(sum_low_copied, 1)

            def query_high(bank, i):
                nc.scalar.activation(query_hi[:, i, :], bank[:, 0 : 2 * P], ACT.Copy).then_inc(query_hi_ready, 1)

            def keys_high(c):
                cs = slice(c * CHUNK, (c + 1) * CHUNK)
                act.wait_ge(raw_keys_landed[c], 16)
                nc.scalar.activation(keys_hi[:, cs], raw[:, cs], ACT.Copy).then_inc(keys_hi_ready, 1)

            act.wait_ge(queries_made, 1)
            query_high(turn_ps[0], 0)
            keys_high(0)
            act.wait_ge(consts_ready, 2)
            for c in range(CHUNKS):
                mask(0, 2 * c)
                if c + 1 < CHUNKS:
                    keys_high(c + 1)
                mask(0, 2 * c + 1)
                if c == 2:
                    act.wait_ge(queries_made, 2)
                    query_high(turn_ps[1], 1)
            mask(0, UNITS)
            exp(0, 0)
            exp(0, 1)
            mask(0, UNITS + 1)
            mask(0, LEAD)

            def step(it, r):
                now = it * ROUND_STEPS + r if isinstance(it, int) else 0
                if r % STEPS == LAG and r >= STEPS:
                    low_sum(it, r // STEPS)
                if now < ALL_STEPS:
                    high(it, r)
                if r % 4 >= 2:
                    g = LEAD + 2 * (r // 4) + r % 4 - 1
                    if not isinstance(it, int) or it * ROUND * UNITS + g < ALL_UNITS:
                        mask(it, g)
                elif now + 4 < ALL_STEPS:
                    exp(it, 2 * (r // 4 + 1) + r % 4)

            def extra(it, p):
                b = extra_use(p)
                act.wait_ge(turns_made, it * ROUND * BANK_USES + b + 1)
                query_high(turn_ps[b % BANKS], (p + 2) % ROUND)

            for r in range(START):
                step(0, r)
                if r == EXTRA - 1:
                    extra(0, 0)
            with act.Fori(0, ROUNDS - 1) as it:
                for r in range(START, START + ROUND_STEPS):
                    step(it, r)
                    if r % STEPS == EXTRA - 1:
                        extra(it, r // STEPS)
            for r in range(START, ROUND_STEPS):
                step(ROUNDS - 1, r)
            low_sum(ROUNDS - 1, ROUND)

        @block.vector
        def _(dve):
            def wait_scores(it, g):
                dve.wait_ge(scores_made, it * ROUND * UNITS + g + 1)
                dve.wait_ge(mask_ready, it * ROUND * UNITS + g + 1)

            def mask_scores(g):
                p, c, t = g // UNITS % ROUND, g % UNITS // 2, g % 2
                nc.vector.tensor_tensor_reduce(unit(g), score_ps[g % 2][:, :], unit(g), 1.0, -3.0e38,
                                               ALU.subtract, ALU.max,
                                               unit_max[:, p, t, c : c + 1]).then_inc(masked, 1)

            def bias(it, p):
                i = p % ROUND
                dve.wait_ge(masked, (it * ROUND + p + 1) * UNITS)
                nc.vector.tensor_reduce(row_max[:, i, :], unit_max[:, i, :, :], AX_X,
                                        ALU.max).then_inc(row_max_ready, 1)
                dve.wait_ge(row_max_ready, it * ROUND + p + 1)
                nc.vector.tensor_scalar(exp_bias[:, i, :], row_max[:, i, :], -SCALE, None,
                                        ALU.mult).then_inc(exp_bias_ready, 1)

            def low(it, r):
                dve.wait_ge(turned_hi, it * ROUND_STEPS + r + 1)
                hi = turned[:, r % TURNED, :, 0, :].bitcast(F32)
                nc.vector.tensor_tensor(turned[:, r % TURNED, :, 1, :],
                                        turn_ps[use(r) % BANKS][:, :].rearrange("p (i n) -> p i n", i=2),
                                        hi, ALU.subtract).then_inc(turned_both, 1)

            def query_low(bank, i):
                nc.vector.tensor_tensor(query_lo[:, i, :], bank[:, 0 : 2 * P],
                                        query_hi[:, i, :].bitcast(F32), ALU.subtract).then_inc(query_ready, 1)

            def copy_sum(it, p):
                dve.wait_ge(sum_low_copied, it * ROUND + p)
                nc.vector.tensor_tensor(summed_t[:, :], sum_ps[:, 0, :], sum_low[:, :],
                                        ALU.add).then_inc(sum_copied, 1)

            def invert_denom(it, p):
                i = (p - 1) % ROUND
                dve.wait_ge(exp_done, (it * ROUND + p) * UNITS)
                nc.vector.tensor_reduce(denom[:, i, :], unit_sum[:, i, :, :], AX_X,
                                        ALU.add).then_inc(denom_ready, 1)
                dve.wait_ge(denom_ready, it * ROUND + p)
                nc.vector.reciprocal(inv_denom[:, i, :], denom[:, i, :]).then_inc(inv_denom_ready, 1)

            def finish(it, p, b, query):
                i = (p - 1) % ROUND
                bank = turn_ps[b % BANKS]
                if query:
                    dve.wait_ge(query_hi_ready, it * ROUND + p + 3)
                    query_low(bank, (p + 2) % ROUND)
                if p == 0:
                    return
                dve.wait_ge(turns_made, it * ROUND * BANK_USES + b + 1)
                dve.wait_ge(out_free[i], 16 * (it + (p - 1) // ROUND + 1))
                dve.wait_ge(inv_denom_ready, it * ROUND + p)
                dve.wait_ge(x_landed[i], 16 * (it + (p - 1) // ROUND + 1))
                for t in range(2):
                    last = nc.vector.scalar_tensor_tensor(
                        out_sb[:, i, t, :], bank[:, (2 + t) * P : (3 + t) * P], inv_denom[:, i, t : t + 1],
                        x_sb[:, i, t, :], ALU.mult, ALU.add)
                last.then_inc(y_ready, 1)

            def statistics(it, p):
                i = (p - 1) % ROUND
                dve.wait_ge(y_ready, it * ROUND + p)
                for t in range(2):
                    last = nc.vector.bn_stats(stats[:, i, t, :], out_sb[:, i, t, :])
                last.then_inc(stats_ready, 1)

            def wait_statistics(it, p):
                dve.wait_ge(stats_ready, it * ROUND + p)

            def mean_variance(p):
                i = (p - 1) % ROUND
                for t in range(2):
                    last = nc.vector.bn_aggr(mean_var[:, i, t, :], stats[:, i, t, :])
                last.then_inc(mean_var_ready, 1)

            def norm(it, p):
                i = (p - 1) % ROUND
                dve.wait_ge(inv_std_ready, it * ROUND + p)
                for t in range(2):
                    last = nc.vector.tensor_scalar(out_sb[:, i, t, :], out_sb[:, i, t, :], mean_var[:, i, t, 0:1],
                                                   inv_std[:, i, t : t + 1], ALU.subtract, ALU.mult)
                last.then_inc(normed, 1)

            def keys_low(c):
                cs = slice(c * CHUNK, (c + 1) * CHUNK)
                dve.wait_ge(keys_hi_ready, c + 1)
                nc.vector.tensor_tensor(keys_lo[:, cs], raw[:, cs], keys_hi[:, cs].bitcast(F32),
                                        ALU.subtract).then_inc(keys_ready, 1)

            def values_low(c):
                b = slice(c * VALUES, (c + 1) * VALUES)
                dve.wait_ge(values_hi_ready, c + 1)
                nc.vector.tensor_tensor(values_lo[:, b, :], raw_values[:, :, :], values_hi[:, b, :].bitcast(F32),
                                        ALU.subtract).then_inc(values_ready, 1)

            dve.wait_ge(query_hi_ready, 1)
            query_low(turn_ps[0], 0)
            keys_low(0)
            for c in range(CHUNKS):
                wait_scores(0, 2 * c)
                mask_scores(2 * c)
                if c + 1 < CHUNKS:
                    keys_low(c + 1)
                wait_scores(0, 2 * c + 1)
                mask_scores(2 * c + 1)
                if c == 2:
                    dve.wait_ge(query_hi_ready, 2)
                    query_low(turn_ps[1], 1)
            bias(0, 0)
            wait_scores(0, UNITS)
            mask_scores(UNITS)
            values_low(0)
            wait_scores(0, UNITS + 1)
            mask_scores(UNITS + 1)

            def step(it, r):
                now = it * ROUND_STEPS + r if isinstance(it, int) else 0
                p, q = divmod(r, STEPS)
                g = LEAD + r // 2 - (q == 2)
                score = (r % 2 or q == 2) and q != 1 and LEAD + now // 2 < ALL_UNITS
                late = p >= 1
                if q == LAG and late:
                    copy_sum(it, p)
                if score:
                    wait_scores(it, g)
                if q == 8 and late:
                    wait_statistics(it, p)
                low(it, r)
                if score:
                    mask_scores(g)
                    if g % UNITS == UNITS - 1:
                        bias(it, g // UNITS)
                if q == 3 and late:
                    invert_denom(it, p)
                if q == 7 and late:
                    statistics(it, p)
                if q == 8 and late:
                    mean_variance(p)
                if q == 10 and late:
                    norm(it, p)

            for r in range(START):
                step(0, r)
                if r % CHUNK_STEPS == 2:
                    values_low(r // CHUNK_STEPS + 1)
                if r == EXTRA - 1:
                    finish(0, 0, extra_use(0), True)
            with dve.Fori(0, ROUNDS - 1) as it:
                for r in range(START, START + ROUND_STEPS):
                    step(it, r)
                    if r % STEPS == EXTRA - 1:
                        finish(it, r // STEPS, extra_use(r // STEPS), True)
            for r in range(START, ROUND_STEPS):
                step(ROUNDS - 1, r)
                if r % STEPS == EXTRA - 1:
                    finish(ROUNDS - 1, r // STEPS, extra_use(r // STEPS), False)
            copy_sum(ROUNDS - 1, ROUND)
            invert_denom(ROUNDS - 1, ROUND)
            finish(ROUNDS - 1, ROUND, use(ROUND_STEPS), False)
            statistics(ROUNDS - 1, ROUND)
            wait_statistics(ROUNDS - 1, ROUND)
            mean_variance(ROUND)
            norm(ROUNDS - 1, ROUND)

        @block.gpsimd
        def _(pool):
            nc.gpsimd.memset(identity[:, :], 0.0).then_inc(identity_cleared, 1)
            pool.wait_ge(identity_cleared, 1)
            nc.gpsimd.affine_select(out=identity[:, :], in_=identity[:, :], compare_op=ALU.not_equal, fill=1.0,
                                    base=0, pattern=[[-1, P]], channel_multiplier=1).then_inc(consts_ready, 1)
            for i in range(ROUND):
                nc.gpsimd.memset(out_sb[:, i, :, :], 0.0).then_inc(out_free[i], 16)
            nc.gpsimd.memset(minus_half[:, :], -0.5)
            nc.gpsimd.memset(eps[:, :], EPS).then_inc(consts_ready, 1)

            for c in range(CHUNKS):
                pool.wait_ge(raw_values_landed, 16 * (c + 1))
                nc.gpsimd.tensor_scalar(values_hi[:, c * VALUES : (c + 1) * VALUES, :], raw_values[:, :, :],
                                        1.0, 0.0, ALU.mult, ALU.add).then_inc(values_hi_ready, 1)

            def deviation(it, i):
                pool.wait_ge(mean_var_ready, it * ROUND + i + 1)
                nc.gpsimd.tensor_tensor(var_eps[:, i, :], mean_var[:, i, :, 1], eps[:, :],
                                        ALU.add).then_inc(var_eps_ready, 1)
                pool.wait_ge(var_eps_ready, it * ROUND + i + 1)
                nc.gpsimd.tensor_tensor(inv_std[:, i, :], var_eps[:, i, :], minus_half[:, :],
                                        ALU.pow).then_inc(inv_std_ready, 1)

            with pool.Fori(0, ROUNDS) as it:
                for i in range(ROUND):
                    deviation(it, i)


def kernel(x, adj, L0_gnn_input, L0_gnn_weight):
    import numpy as np
    import concourse.bacc as bacc
    from concourse.bass_utils import run_bass_kernel_spmd

    nc = bacc.Bacc("TRN2", target_bir_lowering=False, num_devices=1)
    x, adj, values, weight = (np.asarray(a) for a in (x, adj, L0_gnn_input, L0_gnn_weight))
    arrays = {
        "x": np.ascontiguousarray(x),
        "x_t": np.ascontiguousarray(x.T),
        "adj": np.ascontiguousarray(adj),
        "values": np.ascontiguousarray(values),
        "keys_t": np.ascontiguousarray(values.T),
        "weight": np.ascontiguousarray(weight),
    }
    args = [nc.dram_tensor(f"{n}_dram", a.shape, mybir.dt.from_np(a.dtype), kind="ExternalInput").ap()
            for n, a in arrays.items()]
    out = nc.dram_tensor("out_dram", x.shape, F32, kind="ExternalOutput").ap()
    gnn_attention_norm(nc, *args, out)
    r = run_bass_kernel_spmd(nc, [{f"{n}_dram": a for n, a in arrays.items()}], core_ids=[0])
    return r.results[0]["out_dram"]
```

```python
from contextlib import ExitStack

import concourse.bass as bass
from concourse import mybir

F32 = mybir.dt.float32
F32R = mybir.dt.float32r
I32 = mybir.dt.int32
ALU = mybir.AluOpType
ACT = mybir.ActivationFunctionType
AX_X = mybir.AxisListType.X

TEMPERATURE = 0.07
EPS = 1e-5
BIG = 2.0**100
P = 128


def gnn_attention_norm(nc, x, x_t, adj, values, inputs_t, weight_t, out):
    rows, d = x.shape
    cols = values.shape[0]
    assert d == P and rows % (2 * P) == 0

    CHUNK = 1024
    HALF = 512
    CHUNKS = cols // CHUNK
    PAIRS = rows // (2 * P)
    UNITS = 2 * CHUNKS
    ALL_UNITS = UNITS * PAIRS
    STEPS = cols // 256
    CHUNK_STEPS = CHUNK // 256
    VALUES = CHUNK // P
    ALL_STEPS = STEPS * PAIRS
    SLOTS = 9
    AHEAD = 2
    LEAD = UNITS + AHEAD
    LAG = 2
    TURNED = 4
    BANKS = 3
    ROUND = 3
    ROUND_STEPS = ROUND * STEPS
    ROUNDS = PAIRS // ROUND
    NO_SCORES = ROUND_STEPS - 2 * AHEAD - STEPS
    BACK = 6
    START = 20
    FIRST_USES = STEPS + BACK
    BANK_USES = STEPS + 1
    SCALE = 1.0 / TEMPERATURE
    assert (ROUND * BANK_USES) % BANKS == 0 and (ROUND * CHUNKS) % SLOTS == 0
    assert ROUND_STEPS % TURNED == 0 and PAIRS % ROUND == 0

    def use(r):
        return r + max(0, (r - BACK) // STEPS)

    def back_use(p):
        return use(STEPS * p + BACK) - 1

    values_v = values.rearrange("(b p) n -> p b n", p=P)

    def rows_of(dram, p):
        return dram[bass.ds(p * 2 * P, 2 * P), :]

    with ExitStack() as ctx:

        def sb(name, shape, dt):
            return ctx.enter_context(nc.sbuf_tensor(name, shape, dt))

        def psum(name, shape):
            return ctx.enter_context(nc.psum_tensor(name, shape, F32))

        def sem(name):
            return ctx.enter_context(nc.semaphore(name))

        keys_hi = sb("keys_hi", [P, cols], F32R)
        keys_lo = sb("keys_lo", [P, cols], F32R)
        values_hi = sb("values_hi", [P, cols // P, P], F32R)
        values_lo = sb("values_lo", [P, cols // P, P], F32R)
        ring = sb("ring", [P, SLOTS, 2, CHUNK], I32)
        turned = sb("turned", [P, TURNED, 2, 2, 2 * P], F32R)
        query_hi = sb("query_hi", [P, ROUND, 2 * P], F32R)
        query_lo = sb("query_lo", [P, ROUND, 2 * P], F32R)
        raw_values = sb("raw_values", [P, VALUES, P], F32)
        weight_sb = sb("weight_sb", [P, P], F32)
        identity = sb("identity", [P, P], F32)
        xt_sb = sb("xt_sb", [P, ROUND, 2 * P], F32)
        x_sb = sb("x_sb", [P, ROUND, 2, P], F32)
        out_sb = sb("out_sb", [P, ROUND, 2, P], F32)
        sum_low = sb("sum_low", [P, 2 * P], F32)
        summed_t = sb("summed_t", [P, 2 * P], F32)
        unit_max = sb("unit_max", [P, ROUND, 2, CHUNKS], F32)
        unit_sum = sb("unit_sum", [P, ROUND, 2, CHUNKS], F32)
        row_max = sb("row_max", [P, ROUND, 2], F32)
        exp_bias = sb("exp_bias", [P, ROUND, 2], F32)
        denom = sb("denom", [P, ROUND, 2], F32)
        inv_denom = sb("inv_denom", [P, ROUND, 2], F32)
        stats = sb("stats", [P, ROUND, 2, 6], F32)
        mean_var = sb("mean_var", [P, ROUND, 2, 2], F32)
        var_eps = sb("var_eps", [P, ROUND, 2], F32)
        inv_std = sb("inv_std", [P, ROUND, 2], F32)
        minus_half = sb("minus_half", [P, 2], F32)
        eps = sb("eps", [P, 2], F32)

        score_ps = [psum(f"score_ps{i}", [P, CHUNK]) for i in range(2)]
        turn_ps = [psum(f"turn_ps{i}", [P, HALF]) for i in range(BANKS)]
        sum_ps = psum("sum_ps", [P, 2, 2 * P])

        inputs = ring[:, CHUNKS:SLOTS, :, :].bitcast(F32).rearrange("p s a n -> p (s a n)")

        weight_landed = sem("weight_landed")
        inputs_landed = [sem(f"inputs_landed{c}") for c in range(CHUNKS)]
        raw_values_landed = sem("raw_values_landed")
        adj_landed = [sem(f"adj_landed{s}") for s in range(SLOTS)]
        xt_landed = [sem(f"xt_landed{i}") for i in range(ROUND)]
        x_landed = [sem(f"x_landed{i}") for i in range(ROUND)]
        out_free = [sem(f"out_free{i}") for i in range(ROUND)]
        consts_ready = sem("consts_ready")
        keys_made = sem("keys_made")
        keys_hi_ready = sem("keys_hi_ready")
        keys_ready = sem("keys_ready")
        values_hi_ready = sem("values_hi_ready")
        values_ready = sem("values_ready")
        query_hi_ready = sem("query_hi_ready")
        query_ready = sem("query_ready")
        scores_made = sem("scores_made")
        mask_ready = sem("mask_ready")
        masked = sem("masked")
        row_max_ready = sem("row_max_ready")
        exp_bias_ready = sem("exp_bias_ready")
        exp_done = sem("exp_done")
        turns_made = sem("turns_made")
        turned_hi = sem("turned_hi")
        turned_both = sem("turned_both")
        steps_summed = sem("steps_summed")
        sum_low_copied = sem("sum_low_copied")
        sum_copied = sem("sum_copied")
        denom_ready = sem("denom_ready")
        inv_denom_ready = sem("inv_denom_ready")
        y_ready = sem("y_ready")
        stats_ready = sem("stats_ready")
        mean_var_ready = sem("mean_var_ready")
        identity_cleared = sem("identity_cleared")
        var_eps_ready = sem("var_eps_ready")
        inv_std_ready = sem("inv_std_ready")
        normed = sem("normed")

        def unit(g):
            return ring[:, g // 2 % SLOTS, g % 2, :].bitcast(F32)

        block = ctx.enter_context(nc.Block())

        @block.sync
        def _(sp):
            sp.dma_start(weight_sb[:, :], weight_t).then_inc(weight_landed, 16)

            def load_xt(p, i):
                sp.dma_start(xt_sb[:, i, :], x_t[:, bass.ds(p * 2 * P, 2 * P)]).then_inc(xt_landed[i], 16)

            def load_x(p, i):
                src = rows_of(x, p).rearrange("(a p) n -> p a n", p=P)
                sp.dma_start(x_sb[:, i, :, :], src).then_inc(x_landed[i], 16)

            def load_adj(p, k):
                c = k % CHUNKS
                src = rows_of(adj, p)[:, c * CHUNK : (c + 1) * CHUNK].rearrange("(a p) n -> p a n", p=P)
                sp.dma_start(ring[:, k % SLOTS, :, :], src).then_inc(adj_landed[k % SLOTS], 16)

            def store(p, i, count):
                sp.wait_ge(normed, count)
                dst = rows_of(out, p).rearrange("(a p) n -> p a n", p=P)
                sp.dma_start(dst, out_sb[:, i, :, :]).then_inc(out_free[i], 16)

            def load_values(c):
                if c:
                    sp.wait_ge(values_ready, c)
                sp.dma_start(raw_values[:, :, :],
                             values_v[:, c * VALUES : (c + 1) * VALUES, :]).then_inc(raw_values_landed, 16)

            def load_inputs(c):
                cs = slice(c * CHUNK, (c + 1) * CHUNK)
                sp.dma_start(inputs[:, cs], inputs_t[:, cs]).then_inc(inputs_landed[c], 16)

            load_inputs(0)
            load_xt(0, 0)
            for c in range(CHUNKS):
                if c + 1 < CHUNKS:
                    load_inputs(c + 1)
                load_adj(0, c)
                if c == 0:
                    load_xt(1, 1)
            for i in range(SLOTS - CHUNKS):
                sp.wait_ge(keys_made, 4 * i + 4)
                load_adj(1, CHUNKS + i)
                if i == 0:
                    load_values(0)
            load_values(1)
            load_xt(2, 2)
            load_x(0, 0)
            load_x(1, 1)

            def chunk(it, i):
                k = SLOTS + i
                p = it * ROUND + k // CHUNKS
                sp.wait_ge(turns_made, it * (ROUND * BANK_USES) + use(CHUNK_STEPS * i + CHUNK_STEPS - 1) + 1)
                load_adj(p, k)

            def pair_io(it, i):
                q, c = divmod(i, CHUNKS)
                p = it * ROUND + q
                static = isinstance(it, int)
                if c == CHUNKS - 2 and not (static and p == 0):
                    store(p - 1, (q - 1) % ROUND, p)
                if c == CHUNKS - 1:
                    if not static or p + 3 < PAIRS:
                        load_xt(p + 3, q % ROUND)
                    if not static or p + 2 < PAIRS:
                        load_x(p + 2, (q + 2) % ROUND)

            body = ROUND * CHUNKS
            first = CHUNKS - 1
            for i in range(first):
                if i + 2 < CHUNKS:
                    load_values(i + 2)
                chunk(0, i)
                pair_io(0, i)
            with sp.Fori(0, ROUNDS - 1) as it:
                for i in range(first, first + body):
                    chunk(it, i)
                    pair_io(it, i)
            for i in range(first, body):
                if (ROUNDS - 1) * body + SLOTS + i < PAIRS * CHUNKS:
                    chunk(ROUNDS - 1, i)
                pair_io(ROUNDS - 1, i)
            store(PAIRS - 1, (PAIRS - 1) % ROUND, PAIRS)
            for i in range(ROUND):
                sp.wait_ge(out_free[i], 16 * (ROUNDS + 1))

        @block.tensor
        def _(pe):
            def scores(it, r, halves=(0, 1)):
                g = LEAD + r // 2
                p, c, t = g // UNITS, g % UNITS // 2, g % 2
                q_hi = query_hi[:, p % ROUND, t * P : (t + 1) * P]
                q_lo = query_lo[:, p % ROUND, t * P : (t + 1) * P]
                for h in halves:
                    if h == 0:
                        if g >= 2:
                            pe.wait_ge(masked, it * ROUND * UNITS + g - 1)
                        if g % UNITS == 0:
                            pe.wait_ge(query_ready, it * ROUND + p + 1)
                    n0 = c * CHUNK + h * HALF
                    k_hi, k_lo = keys_hi[:, n0 : n0 + HALF], keys_lo[:, n0 : n0 + HALF]
                    to = score_ps[g % 2][:, h * HALF : (h + 1) * HALF]
                    pe.matmul(to, q_hi, k_hi, start=True, stop=False)
                    pe.matmul(to, q_hi, k_lo, start=False, stop=False)
                    last = pe.matmul(to, q_lo, k_hi, start=False, stop=True)
                if h == 1:
                    last.then_inc(scores_made, 1)

            def turn(it, r):
                p, q = divmod(r, STEPS)
                c = q // CHUNK_STEPS
                if q % CHUNK_STEPS == 0:
                    pe.wait_ge(exp_done, it * ROUND * UNITS + UNITS * p + 2 * c + 2)
                b = use(r)
                if b - BANKS >= 0:
                    free_bank(it, b - BANKS)
                for i in range(2):
                    n0 = (2 * (q % CHUNK_STEPS) + i) * P
                    for t in range(2):
                        last = pe.transpose(turn_ps[b % BANKS][:, (2 * i + t) * P : (2 * i + t + 1) * P],
                                            unit(UNITS * p + 2 * c + t)[:, n0 : n0 + P], identity[:, :])
                last.then_inc(turns_made, 1)

            def free_bank(it, b):
                p, q = divmod(b - FIRST_USES, BANK_USES)
                if b >= FIRST_USES and q == 0:
                    pe.wait_ge(y_ready, it * ROUND + p + 1)
                else:
                    r = b if b < FIRST_USES else FIRST_USES + STEPS * p + q - 1
                    pe.wait_ge(turned_both, it * ROUND_STEPS + r + 1)

            def sum_values(it, r):
                q = r % STEPS
                if q == 0:
                    pe.wait_ge(sum_copied, it * ROUND + r // STEPS)
                pe.wait_ge(turned_both, it * ROUND_STEPS + r + 1)
                if isinstance(it, int) and it == 0 and q % CHUNK_STEPS == 0:
                    pe.wait_ge(values_ready, q // CHUNK_STEPS + 1)
                for i in range(2):
                    probs = turned[:, r % TURNED, i, :, :]
                    n = 2 * q + i
                    first, end = n == 0, n == cols // P - 1
                    pe.matmul(sum_ps[:, :, :], values_hi[:, n, :], probs, start=first, stop=False)
                    last = pe.matmul(sum_ps[:, 0, :], values_lo[:, n, :], probs[:, 0, :], start=False, stop=end)
                last.then_inc(steps_summed, 1)

            def turn_back(it, p, b=None):
                b = back_use(p) if b is None else b
                free_bank(it, b - BANKS)
                pe.wait_ge(sum_copied, it * ROUND + p)
                for t in range(2):
                    last = pe.transpose(turn_ps[b % BANKS][:, t * P : (t + 1) * P],
                                        summed_t[:, t * P : (t + 1) * P], identity[:, :])
                last.then_inc(turns_made, 1)

            def make_keys(h):
                if h % 2 == 0:
                    pe.wait_ge(inputs_landed[h // 2], 16)
                if h >= BANKS:
                    pe.wait_ge(keys_ready, h - BANKS + 1)
                pe.matmul(turn_ps[h % BANKS][:, :], weight_sb[:, :], inputs[:, h * HALF : (h + 1) * HALF],
                          start=True, stop=True).then_inc(keys_made, 1)

            pe.wait_ge(weight_landed, 16)
            for h in range(4):
                make_keys(h)
            for g in range(LEAD):
                for h in range(2):
                    if g % 2 == 0 and g < UNITS:
                        pe.wait_ge(keys_ready, g + h + 1)
                    scores(0, 2 * (g - LEAD), (h,))
                if g % 2 and g + 3 < UNITS:
                    make_keys(g + 3)
                    make_keys(g + 4)
            pe.wait_ge(consts_ready, 2)

            def step(it, r):
                turn(it, r)
                if r % STEPS == LAG + 1:
                    sum_values(it, r - LAG - 1)
                scores(it, r, (r % 2,))
                if r >= LAG and r % STEPS != LAG:
                    sum_values(it, r - LAG)

            def scoreless_step(it, r):
                if r < ROUND_STEPS:
                    turn(it, r)
                if r > NO_SCORES:
                    sum_values(it, r - LAG - 1)

            for r in range(START):
                step(0, r)
            pe.wait_ge(values_ready, CHUNKS)
            with pe.Fori(0, ROUNDS - 1) as it:
                for r in range(START, START + ROUND_STEPS):
                    step(it, r)
                    if r % STEPS == BACK - 1:
                        turn_back(it, r // STEPS)
            for r in range(START, ROUND_STEPS + LAG + 1):
                (step if r < NO_SCORES else scoreless_step)(ROUNDS - 1, r)
                if r % STEPS == BACK - 1:
                    turn_back(ROUNDS - 1, r // STEPS)
            turn_back(ROUNDS - 1, ROUND, use(ROUND_STEPS))

        @block.scalar
        def _(act):
            def mask(it, g):
                k = g // 2
                slot = k % SLOTS
                if g % 2 == 0:
                    act.wait_ge(adj_landed[slot], it * 16 * (ROUND * CHUNKS // SLOTS) + 16 * (k // SLOTS + 1))
                nc.scalar.activation(unit(g), ring[:, slot, g % 2, :], ACT.Relu,
                                     bias=BIG, scale=-BIG).then_inc(mask_ready, 1)

            def exp(it, g):
                p, c, t = g // UNITS % ROUND, g % UNITS // 2, g % 2
                if g % UNITS == 0:
                    act.wait_ge(exp_bias_ready, it * ROUND + g // UNITS + 1)
                nc.scalar.activation(unit(g), unit(g), ACT.Exp, bias=exp_bias[:, p, t : t + 1], scale=SCALE,
                                     accum_out=unit_sum[:, p, t, c : c + 1]).then_inc(exp_done, 1)

            def high(it, r):
                b = use(r)
                if r >= TURNED:
                    act.wait_ge(steps_summed, it * ROUND_STEPS + r - TURNED + 1)
                act.wait_ge(turns_made, it * ROUND * BANK_USES + b + 1)
                nc.scalar.activation(turned[:, r % TURNED, :, 0, :],
                                     turn_ps[b % BANKS][:, :].rearrange("p (i n) -> p i n", i=2),
                                     ACT.Copy).then_inc(turned_hi, 1)

            def low_sum(it, p):
                act.wait_ge(steps_summed, it * ROUND_STEPS + STEPS * p)
                nc.scalar.activation(sum_low[:, :], sum_ps[:, 1, :], ACT.Copy).then_inc(sum_low_copied, 1)

            def keys_high(h):
                act.wait_ge(keys_made, h + 1)
                nc.scalar.activation(keys_hi[:, h * HALF : (h + 1) * HALF], turn_ps[h % BANKS][:, :],
                                     ACT.Copy).then_inc(keys_hi_ready, 1)

            for h in range(4):
                keys_high(h)
            for c in range(CHUNKS):
                mask(0, 2 * c)
                mask(0, 2 * c + 1)
                if c + 2 < CHUNKS:
                    keys_high(2 * c + 4)
                    keys_high(2 * c + 5)
            mask(0, UNITS)
            mask(0, UNITS + 1)
            exp(0, 0)
            exp(0, 1)
            mask(0, LEAD)

            def step(it, r):
                now = it * ROUND_STEPS + r if isinstance(it, int) else 0
                if r % STEPS == LAG and r >= STEPS:
                    low_sum(it, r // STEPS)
                if now < ALL_STEPS:
                    high(it, r)
                if r % 4 >= 2:
                    g = LEAD + 2 * (r // 4) + r % 4 - 1
                    if not isinstance(it, int) or it * ROUND * UNITS + g < ALL_UNITS:
                        mask(it, g)
                elif now + 4 < ALL_STEPS:
                    exp(it, 2 * (r // 4 + 1) + r % 4)

            for r in range(START):
                step(0, r)
            with act.Fori(0, ROUNDS - 1) as it:
                for r in range(START, START + ROUND_STEPS):
                    step(it, r)
            for r in range(START, ROUND_STEPS):
                step(ROUNDS - 1, r)
            low_sum(ROUNDS - 1, ROUND)

        @block.vector
        def _(dve):
            def wait_scores(it, g):
                dve.wait_ge(scores_made, it * ROUND * UNITS + g + 1)
                dve.wait_ge(mask_ready, it * ROUND * UNITS + g + 1)

            def mask_scores(g):
                p, c, t = g // UNITS % ROUND, g % UNITS // 2, g % 2
                nc.vector.tensor_tensor_reduce(unit(g), score_ps[g % 2][:, :], unit(g), 1.0, -3.0e38,
                                               ALU.subtract, ALU.max,
                                               unit_max[:, p, t, c : c + 1]).then_inc(masked, 1)

            def bias(it, p):
                i = p % ROUND
                dve.wait_ge(masked, (it * ROUND + p + 1) * UNITS)
                nc.vector.tensor_reduce(row_max[:, i, :], unit_max[:, i, :, :], AX_X,
                                        ALU.max).then_inc(row_max_ready, 1)
                dve.wait_ge(row_max_ready, it * ROUND + p + 1)
                nc.vector.tensor_scalar(exp_bias[:, i, :], row_max[:, i, :], -SCALE, None,
                                        ALU.mult).then_inc(exp_bias_ready, 1)

            def low(it, r):
                dve.wait_ge(turned_hi, it * ROUND_STEPS + r + 1)
                hi = turned[:, r % TURNED, :, 0, :].bitcast(F32)
                nc.vector.tensor_tensor(turned[:, r % TURNED, :, 1, :],
                                        turn_ps[use(r) % BANKS][:, :].rearrange("p (i n) -> p i n", i=2),
                                        hi, ALU.subtract).then_inc(turned_both, 1)

            def copy_sum(it, p):
                dve.wait_ge(sum_low_copied, it * ROUND + p)
                nc.vector.tensor_tensor(summed_t[:, :], sum_ps[:, 0, :], sum_low[:, :],
                                        ALU.add).then_inc(sum_copied, 1)

            def invert_denom(it, p):
                i = (p - 1) % ROUND
                dve.wait_ge(exp_done, (it * ROUND + p) * UNITS)
                nc.vector.tensor_reduce(denom[:, i, :], unit_sum[:, i, :, :], AX_X,
                                        ALU.add).then_inc(denom_ready, 1)
                dve.wait_ge(denom_ready, it * ROUND + p)
                nc.vector.reciprocal(inv_denom[:, i, :], denom[:, i, :]).then_inc(inv_denom_ready, 1)

            def add_rows(it, p, b=None):
                i = (p - 1) % ROUND
                b = back_use(p) if b is None else b
                bank = turn_ps[b % BANKS]
                dve.wait_ge(turns_made, it * ROUND * BANK_USES + b + 1)
                dve.wait_ge(out_free[i], 16 * (it + (p - 1) // ROUND + 1))
                dve.wait_ge(inv_denom_ready, it * ROUND + p)
                dve.wait_ge(x_landed[i], 16 * (it + (p - 1) // ROUND + 1))
                for t in range(2):
                    last = nc.vector.scalar_tensor_tensor(
                        out_sb[:, i, t, :], bank[:, t * P : (t + 1) * P], inv_denom[:, i, t : t + 1],
                        x_sb[:, i, t, :], ALU.mult, ALU.add)
                last.then_inc(y_ready, 1)

            def statistics(it, p):
                i = (p - 1) % ROUND
                dve.wait_ge(y_ready, it * ROUND + p)
                for t in range(2):
                    last = nc.vector.bn_stats(stats[:, i, t, :], out_sb[:, i, t, :])
                last.then_inc(stats_ready, 1)

            def wait_statistics(it, p):
                dve.wait_ge(stats_ready, it * ROUND + p)

            def mean_variance(p):
                i = (p - 1) % ROUND
                for t in range(2):
                    last = nc.vector.bn_aggr(mean_var[:, i, t, :], stats[:, i, t, :])
                last.then_inc(mean_var_ready, 1)

            def norm(it, p):
                i = (p - 1) % ROUND
                dve.wait_ge(inv_std_ready, it * ROUND + p)
                for t in range(2):
                    last = nc.vector.tensor_scalar(out_sb[:, i, t, :], out_sb[:, i, t, :], mean_var[:, i, t, 0:1],
                                                   inv_std[:, i, t : t + 1], ALU.subtract, ALU.mult)
                last.then_inc(normed, 1)

            def keys_low(h):
                hs = slice(h * HALF, (h + 1) * HALF)
                dve.wait_ge(keys_hi_ready, h + 1)
                nc.vector.tensor_tensor(keys_lo[:, hs], turn_ps[h % BANKS][:, :], keys_hi[:, hs].bitcast(F32),
                                        ALU.subtract).then_inc(keys_ready, 1)

            def values_low(c):
                b = slice(c * VALUES, (c + 1) * VALUES)
                dve.wait_ge(values_hi_ready, c + 1)
                nc.vector.tensor_tensor(values_lo[:, b, :], raw_values[:, :, :], values_hi[:, b, :].bitcast(F32),
                                        ALU.subtract).then_inc(values_ready, 1)

            for h in range(4):
                keys_low(h)
            for c in range(CHUNKS):
                for g in (2 * c, 2 * c + 1):
                    wait_scores(0, g)
                    mask_scores(g)
                if c + 2 < CHUNKS:
                    keys_low(2 * c + 4)
                    keys_low(2 * c + 5)
            bias(0, 0)
            wait_scores(0, UNITS)
            mask_scores(UNITS)
            values_low(0)
            wait_scores(0, UNITS + 1)
            mask_scores(UNITS + 1)

            def step(it, r):
                now = it * ROUND_STEPS + r if isinstance(it, int) else 0
                p, q = divmod(r, STEPS)
                g = LEAD + r // 2 - (q == 2)
                score = (r % 2 or q == 2) and q != 1 and LEAD + now // 2 < ALL_UNITS
                late = p >= 1
                if q == LAG and late:
                    copy_sum(it, p)
                if score:
                    wait_scores(it, g)
                if q == 8 and late:
                    wait_statistics(it, p)
                low(it, r)
                if score:
                    mask_scores(g)
                    if g % UNITS == UNITS - 1:
                        bias(it, g // UNITS)
                if q == 3 and late:
                    invert_denom(it, p)
                if q == 7 and late:
                    statistics(it, p)
                if q == 8 and late:
                    mean_variance(p)
                if q == 10 and late:
                    norm(it, p)

            for r in range(START):
                step(0, r)
                if r % CHUNK_STEPS == 2:
                    values_low(r // CHUNK_STEPS + 1)
            with dve.Fori(0, ROUNDS - 1) as it:
                for r in range(START, START + ROUND_STEPS):
                    step(it, r)
                    if r % STEPS == BACK - 1:
                        add_rows(it, r // STEPS)
            for r in range(START, ROUND_STEPS):
                step(ROUNDS - 1, r)
                if r % STEPS == BACK - 1:
                    add_rows(ROUNDS - 1, r // STEPS)
            invert_denom(ROUNDS - 1, ROUND)
            copy_sum(ROUNDS - 1, ROUND)
            add_rows(ROUNDS - 1, ROUND, use(ROUND_STEPS))
            statistics(ROUNDS - 1, ROUND)
            wait_statistics(ROUNDS - 1, ROUND)
            mean_variance(ROUND)
            norm(ROUNDS - 1, ROUND)

        @block.gpsimd
        def _(pool):
            def query_high(i):
                nc.gpsimd.tensor_scalar(query_hi[:, i, :], xt_sb[:, i, :], 1.0, 0.0, ALU.mult,
                                        ALU.add).then_inc(query_hi_ready, 1)

            def query_low(it, p):
                i = p % ROUND
                pool.wait_ge(query_hi_ready, it * ROUND + p + 1)
                nc.gpsimd.tensor_tensor(query_lo[:, i, :], xt_sb[:, i, :], query_hi[:, i, :].bitcast(F32),
                                        ALU.subtract).then_inc(query_ready, 1)

            def first_query(p):
                pool.wait_ge(xt_landed[p], 16)
                query_high(p)
                query_low(0, p)

            def values_high(c):
                pool.wait_ge(raw_values_landed, 16 * (c + 1))
                nc.gpsimd.tensor_scalar(values_hi[:, c * VALUES : (c + 1) * VALUES, :], raw_values[:, :, :],
                                        1.0, 0.0, ALU.mult, ALU.add).then_inc(values_hi_ready, 1)

            first_query(0)
            nc.gpsimd.memset(identity[:, :], 0.0).then_inc(identity_cleared, 1)
            pool.wait_ge(identity_cleared, 1)
            nc.gpsimd.affine_select(out=identity[:, :], in_=identity[:, :], compare_op=ALU.not_equal, fill=1.0,
                                    base=0, pattern=[[-1, P]], channel_multiplier=1).then_inc(consts_ready, 1)
            for i in range(ROUND):
                nc.gpsimd.memset(out_sb[:, i, :, :], 0.0).then_inc(out_free[i], 16)
            nc.gpsimd.memset(minus_half[:, :], -0.5)
            nc.gpsimd.memset(eps[:, :], EPS).then_inc(consts_ready, 1)
            first_query(1)
            values_high(0)
            values_high(1)
            first_query(2)
            for c in range(2, CHUNKS):
                values_high(c)

            def pair(it, i, query):
                pool.wait_ge(mean_var_ready, it * ROUND + i + 1)
                if query:
                    pool.wait_ge(xt_landed[i], 16 * (it + 2))
                    pool.wait_ge(scores_made, (it * ROUND + i + 1) * UNITS)
                nc.gpsimd.tensor_tensor(var_eps[:, i, :], mean_var[:, i, :, 1], eps[:, :],
                                        ALU.add).then_inc(var_eps_ready, 1)
                pool.wait_ge(var_eps_ready, it * ROUND + i + 1)
                nc.gpsimd.tensor_tensor(inv_std[:, i, :], var_eps[:, i, :], minus_half[:, :],
                                        ALU.pow).then_inc(inv_std_ready, 1)
                if query:
                    query_high(i)
                    query_low(it, ROUND + i)

            with pool.Fori(0, ROUNDS - 1) as it:
                for i in range(ROUND):
                    pair(it, i, True)
            for i in range(ROUND):
                pair(ROUNDS - 1, i, False)


def kernel(x, adj, L0_gnn_input, L0_gnn_weight):
    import numpy as np
    import concourse.bacc as bacc
    from concourse.bass_utils import run_bass_kernel_spmd

    nc = bacc.Bacc("TRN2", target_bir_lowering=False, num_devices=1)
    x, adj, values, weight = (np.asarray(a) for a in (x, adj, L0_gnn_input, L0_gnn_weight))
    arrays = {
        "x": np.ascontiguousarray(x),
        "x_t": np.ascontiguousarray(x.T),
        "adj": np.ascontiguousarray(adj),
        "values": np.ascontiguousarray(values),
        "inputs_t": np.ascontiguousarray(values.T),
        "weight_t": np.ascontiguousarray(weight.T),
    }
    args = [nc.dram_tensor(f"{n}_dram", a.shape, mybir.dt.from_np(a.dtype), kind="ExternalInput").ap()
            for n, a in arrays.items()]
    out = nc.dram_tensor("out_dram", x.shape, F32, kind="ExternalOutput").ap()
    gnn_attention_norm(nc, *args, out)
    r = run_bass_kernel_spmd(nc, [{f"{n}_dram": a for n, a in arrays.items()}], core_ids=[0])
    return r.results[0]["out_dram"]
```
